# Optimizing a Trainium2 kernel written in Bass

```python
import numpy as np
import jax
import jax.numpy as jnp

def _softmax(x, axis=-1):
    return jax.nn.softmax(x, axis=axis)

def _gelu(x):
    return jax.nn.gelu(x, approximate=True)

def _silu(x):
    return jax.nn.silu(x)

def _sigmoid(x):
    return jax.nn.sigmoid(x)

def _layernorm(x, axis=-1, eps=1e-05):
    m = jnp.mean(x, axis=axis, keepdims=True)
    v = jnp.var(x, axis=axis, keepdims=True)
    return (x - m) / jnp.sqrt(v + eps)

def _scatter_add(tgt, idx, src, axis=0):
    return tgt.at[idx].add(src)

def _segment_sum(src, seg, n):
    return jax.ops.segment_sum(src, seg, n)
kernel_name = 'mk_adj_preln_d2_adj_r2_9ce8bd'

def setup_inputs(seed: int=0):
    np.random.seed(seed)
    _w = jnp.asarray

    def _rec_inputs():
        import jax
        import jax.numpy as jnp
        _gk = jax.random.key(seed)
        x = 7.22e-05 + 1 * jax.random.normal(jax.random.fold_in(_gk, 1), (2048, 512), jnp.float32)
        _a = jax.random.bernoulli(jax.random.fold_in(_gk, 2), 0.00390625, (2048, 2048))
        _a = jnp.logical_or(_a, jnp.swapaxes(_a, -1, -2))
        _a = jnp.logical_or(_a, jnp.eye(2048, dtype=bool))
        _af = _a.astype(jnp.float32)
        _d = jnp.maximum(_af.sum(-1), 1.0) ** (-0.5)
        _af = _af * _d[..., :, None] * _d[..., None, :]
        adj = _af
        return (x, adj)
    x, adj = _rec_inputs()

    def _L0_gnn_setup():
        import jax, jax.numpy as jnp
        import numpy as np
        N = 4096
        D = 512

        def adjacent_mat(adj):
            adj = adj + jnp.eye(adj.shape[0], dtype=adj.dtype)
            deg = jnp.sum(adj, axis=1)
            dinv = jnp.where(deg > 0, deg ** (-0.5), 0.0).astype(adj.dtype)
            return dinv[:, None] * adj * dinv[None, :]
        key = jax.random.key(seed)
        k1, k2 = jax.random.split(key)
        x = jax.random.normal(k1, (N, D), dtype=jnp.float32)
        Coefficient2 = 1e-08 * jnp.ones((N, N), dtype=jnp.float32)
        A = jax.random.uniform(k2, (N, N), dtype=jnp.float32)
        return {'x': x, 'Coefficient2': Coefficient2, 'A': A}
    _L0_gnn_all = _L0_gnn_setup()
    _L0_gnn_in = {k: v for k, v in _L0_gnn_all.items() if k in ()}
    del _L0_gnn_all

    def _L1_gnn_setup():
        import jax, jax.numpy as jnp
        import numpy as np
        NBITS = 4
        N_NODES = 4096
        IN_F = 512
        OUT_F = 512

        def _act_quant(x, alpha, b):
            n = float(2 ** b - 1)
            xd = x / alpha
            xc = jnp.minimum(xd, 1.0)
            xq = jnp.round(xc * n) / n
            return xq * alpha

        def _weight_quant(w, alpha, b):
            n = float(2 ** b - 1)
            wd = w / alpha
            wc = jnp.clip(wd, -1.0, 1.0)
            wq = jnp.round(jnp.abs(wc) * n) / n * jnp.sign(wc)
            return wq * alpha
        key = jax.random.key(seed)
        k1, k2, k3 = jax.random.split(key, 3)
        stdv = 1.0 / np.sqrt(OUT_F)
        inp = {'input': jax.random.uniform(k1, (N_NODES, IN_F), dtype=jnp.float32), 'adj': jax.random.uniform(k2, (N_NODES, N_NODES), dtype=jnp.float32), 'adj_scaling_factor': jnp.float32(2.0), 'weight': jax.random.uniform(k3, (IN_F, OUT_F), minval=-stdv, maxval=stdv, dtype=jnp.float32), 'wgt_alpha': jnp.float32(3.0), 'act_alpha': jnp.float32(1.0), 'act_alpha2': jnp.float32(1.0)}
        return inp
    _L1_gnn_all = _L1_gnn_setup()
    _L1_gnn_in = {k: v for k, v in _L1_gnn_all.items() if k in ('adj_scaling_factor', 'weight', 'wgt_alpha', 'act_alpha', 'act_alpha2')}
    del _L1_gnn_all
    return {'x': x, 'adj': adj, 'L1_gnn_adj_scaling_factor': _L1_gnn_in['adj_scaling_factor'], 'L1_gnn_weight': _L1_gnn_in['weight'], 'L1_gnn_wgt_alpha': _L1_gnn_in['wgt_alpha'], 'L1_gnn_act_alpha': _L1_gnn_in['act_alpha'], 'L1_gnn_act_alpha2': _L1_gnn_in['act_alpha2']}

def reference(x, adj, L1_gnn_adj_scaling_factor, L1_gnn_weight, L1_gnn_wgt_alpha, L1_gnn_act_alpha, L1_gnn_act_alpha2):
    import jax
    import jax.numpy as jnp

    def _L0_gnn_ref(x, Coefficient2, A):
        import jax, jax.numpy as jnp
        import numpy as np
        N = 4096
        D = 512

        def adjacent_mat(adj):
            adj = adj + jnp.eye(adj.shape[0], dtype=adj.dtype)
            deg = jnp.sum(adj, axis=1)
            dinv = jnp.where(deg > 0, deg ** (-0.5), 0.0).astype(adj.dtype)
            return dinv[:, None] * adj * dinv[None, :]
        A_c = jax.lax.stop_gradient(A)
        adj = adjacent_mat((A_c + A_c.T) * 0.5)
        y = Coefficient2 @ adj
        y = y @ x
        return y

    def _L1_gnn_ref(input, adj, adj_scaling_factor, weight, wgt_alpha, act_alpha, act_alpha2):
        import jax, jax.numpy as jnp
        import numpy as np
        NBITS = 4
        N_NODES = 4096
        IN_F = 512
        OUT_F = 512

        def _act_quant(x, alpha, b):
            n = float(2 ** b - 1)
            xd = x / alpha
            xc = jnp.minimum(xd, 1.0)
            xq = jnp.round(xc * n) / n
            return xq * alpha

        def _weight_quant(w, alpha, b):
            n = float(2 ** b - 1)
            wd = w / alpha
            wc = jnp.clip(wd, -1.0, 1.0)
            wq = jnp.round(jnp.abs(wc) * n) / n * jnp.sign(wc)
            return wq * alpha
        bit = NBITS
        wb = bit - 1
        mean = jax.lax.stop_gradient(jnp.mean(weight))
        std = jax.lax.stop_gradient(jnp.std(weight, ddof=1))
        w_norm = (weight - mean) / std
        weight_q = _weight_quant(w_norm, wgt_alpha, wb)
        x = _act_quant(input, act_alpha, bit)
        wgt_delta = wgt_alpha / (2 ** (bit - 1) - 1)
        act_delta = act_alpha / (2 ** bit - 1)
        support = jnp.matmul(x / act_delta, weight_q / wgt_delta)
        support = support * act_delta * wgt_delta
        support = jax.nn.relu(support)
        support_q = _act_quant(support, act_alpha2, bit)
        support_delta = act_alpha2 / (2 ** bit - 1)
        output = jnp.matmul(adj / adj_scaling_factor, support_q / support_delta)
        return output * adj_scaling_factor * support_delta
    h = jnp.maximum(_layernorm(x, axis=-1), 0.0)
    x = x + _L0_gnn_ref(h, adj, adj)
    h = jnp.maximum(_layernorm(x, axis=-1), 0.0)
    x = x + _L1_gnn_ref(h, adj, L1_gnn_adj_scaling_factor, L1_gnn_weight, L1_gnn_wgt_alpha, L1_gnn_act_alpha, L1_gnn_act_alpha2)
    return x

_drawn_inputs = setup_inputs


def setup_inputs(seed=0):
    import zlib

    import numpy as np

    out = dict(_drawn_inputs(seed))
    spreads = {}
    factors = {}
    for name, (base, spread) in spreads.items():
        noise = np.random.default_rng([zlib.crc32(name.encode()), seed]).standard_normal(out[name].shape)
        drawn = base * np.exp(spread * noise) if base else spread * noise
        out[name] = jnp.asarray(drawn.astype(out[name].dtype))
    for name, factor in factors.items():
        out[name] = (out[name] * factor).astype(out[name].dtype)
    return out
```

```python
from contextlib import ExitStack

import concourse.bass as bass
from concourse import mybir

ALU = mybir.AluOpType
ACT = mybir.ActivationFunctionType
AX_X = mybir.AxisListType.X
F32 = mybir.dt.float32
F32R = mybir.dt.float32r
BF16 = mybir.dt.bfloat16

P = 128
GROUP = 4
RING = 2
A_STAGE = 3
STAGE = 4
LN_EPS = 1e-5
ACT_LEVELS = 15.0
WGT_LEVELS = 7.0
ROUND = 12582912.0
FREE = 1
TINY = 2.0 ** -100


def chain_plans(starts):
    plans = {"act": {}, "dve": {}, "pe": {}}
    for j, s in enumerate(starts):
        for eng, parts in (("dve", ((s, 0), (s + 2, 1), (s + 3, 2), (s + 7, 3))),
                           ("act", ((s + 1, 0), (s + 3, 1), (s + 5, 2), (s + 6, 3))),
                           ("pe", ((s + 3, 2), (s + 4, 3)))):
            for k, part in parts:
                plans[eng].setdefault(k, []).append((j, part))
    return plans


def wait_for(eng, sem, value):
    if isinstance(value, int) and value <= 0:
        return
    eng.wait_ge(sem, value)


def gnn_layers_kernel(
    nc: bass.Bass,
    x: bass.AP,
    adj: bass.AP,
    weight: bass.AP,
    params: bass.AP,
    out: bass.AP,
):
    N, D = x.shape
    NB = N // P
    NG = NB // GROUP
    DC = D // P
    GC = GROUP * P
    STEPS = NG * NB
    assert N % (P * GROUP) == 0 and D == 512 and NB == NG * GROUP and DC == GROUP

    u_dram = nc.dram_tensor("u_scratch", [N, D], F32).ap()
    x1_dram = nc.dram_tensor("x1_scratch", [N, D], F32).ap()

    adj_rows = adj.rearrange("(k p) n -> p k n", p=P)
    x_rows = x.rearrange("(k p) d -> p k d", p=P)
    u_rows = u_dram.rearrange("(k p) d -> p k d", p=P)
    x1_rows = x1_dram.rearrange("(k p) d -> p k d", p=P)
    out_rows = out.rearrange("(k p) d -> p k d", p=P)
    w_rows = weight.rearrange("(c p) n -> p c n", p=P)

    plans = chain_plans([1, 3, 5, 7])

    SHELLS = [1, 2, 3, 0]
    PIECES = []
    HELD = []
    for at, t in enumerate(SHELLS):
        PIECES.append((t, t))
        for c in SHELLS[at + 1:]:
            PIECES += [(c, t), (t, c)]
        HELD.append(len(PIECES) - 1)
    FIRST_K = [t * GROUP + r for t in SHELLS for r in range(GROUP)]
    X_BEFORE = {2: [0], 7: [1], 9: [2, 3], 12: [4, 5], 14: [6, 7]}
    assert len(PIECES) == NG * NG and NG == 4

    REST = " ".join(f"S{n}" for n in range(12, NB))
    PE_ORDER = ("P0 P1 P2 P3 P4 P5 P6 P7 P8 S0 P9 S1 P10 P11 S2 S3 P12 S4 P13 S5 P14 S6 P15 S7 "
                f"S8 S9 S10 S11 {REST}")
    ACT_ORDER = ("P0 P1 P2 P3 P4 P5 P6 D0 P7 S0 P8 S1 P9 S2 S3 P10 P11 D1 S4 P12 S5 P13 S6 S7 P14 D2 "
                 f"S8 S9 P15 S10 S11 D3 {REST}")
    DVE_ORDER = ("P0 P1 P2 P3 X0 P4 P5 P6 X1 D0 P7 S0 P8 S1 P9 X2 X3 S2 S3 P10 P11 D1 X4 S4 P12 S5 X5 "
                 f"P13 S6 P14 S7 D2 X6 S8 P15 S9 X7 S10 D3 S11 {REST}")
    POOL_ORDER = ("F0 F1 F2 F3 S0 S1 S2 F4 S3 F5 F6 S4 F7 S5 S6 S7 F8 F9 S8 "
                  "F10 S9 F11 S10 F12 S11 F13 S12 F14 S13 F15 S14 S15")

    def walk(order):
        return [(item[0], int(item[1:])) for item in order.split()]

    LINKS_CHAINS = 7 * GROUP

    with ExitStack() as ctx:
        def sb(name, shape, dt, where=ctx):
            return where.enter_context(nc.sbuf_tensor(name, shape, dt))

        def pb(name, shape, dt):
            return ctx.enter_context(nc.psum_tensor(name, shape, dt))

        def sem(name):
            return ctx.enter_context(nc.semaphore(name))

        adjT = sb("adjT", [P, NB, N], F32)
        with ExitStack() as left:
            vec = sb("vec", [P, NB, D], F32, left)
        sq_wide = sb("sq_wide", [P, NB, D], F32R)
        with ExitStack() as before_wq:
            ones = sb("ones", [P, P], F32, before_wq)
        wq = sb("wq", [P, DC, D], BF16)
        ident16 = sb("ident16", [P, P], BF16)
        par = sb("par", [P, 4], F32)
        ipar = sb("ipar", [P, 4], F32)
        delta = sb("delta", [P, 4], F32)
        levels = sb("levels", [P, 2], F32)
        kappa = sb("kappa", [P, 1], F32)
        dinv = sb("dinv", [P, NB], F32)
        stats = sb("stats", [P, GROUP, 6], F32)
        mv = sb("mv", [P, NB, 2], F32)
        var_ = sb("var_", [P, NB], F32)
        root = sb("root", [P, NB], F32)
        rs = sb("rs", [P, NB], F32)
        newton = sb("newton", [P, NB], F32)
        first_root = sb("first_root", [P, 1], F32)
        nbias = sb("nbias", [P, 1], F32)
        wst = sb("wst", [P, 2 * DC + 2], F32)
        deg = sb("deg", [P, NB], F32)
        halves = sb("halves", [P, 4 * RING, D], F32R)
        hi, lo, vhi, vlo = (halves[:, i * RING:(i + 1) * RING, :] for i in range(4))
        hi_wide, lo_wide = (halves[:, i * 2 * RING:(i + 1) * 2 * RING, :] for i in range(2))
        with ExitStack() as early:
            a_stage = sb("a_stage", [P, A_STAGE, GROUP, GC], F32, early)
            ident32 = sb("ident32", [P, P], F32, early)
            gscale = sb("gscale", [P, NB], F32, early)
            gbias = sb("gbias", [P, NB], F32, early)
            parts = sb("parts", [P, 2 * NG, NB], F32, early)
        rows = sb("rows", [P, GROUP, D], F32)
        h2q = sb("h2q", [P, D], BF16)
        h2qT = sb("h2qT", [P, DC, P], BF16)
        with ExitStack() as first:
            b_stage = sb("b_stage", [P, STAGE, GC], F32, first)
            w_sb = sb("w_sb", [P, DC, D], F32, first)
        sq = sb("sq", [P, NB, D], BF16)

        acc = pb("acc", [P, GROUP, D], F32)
        bank = [pb(f"bank{i}", [P, GC], F32) for i in range(GROUP)]
        sup = bank[0]
        t16 = bank[1][:, :].bitcast(BF16)
        vhi32 = vhi.bitcast(F32)

        def step(phase, q, k):
            return phase * STEPS + q * NB + k

        def held(n):
            r = n % GROUP
            if n < 2 * GROUP:
                return adjT[:, r, 0:GC]
            return a_stage[:, HELD[n // GROUP] % A_STAGE, r, :]

        def half_blocks(half):
            start = SHELLS[half // 2] * GROUP + half % 2 * (GROUP // 2)
            return slice(start, start + GROUP // 2)

        def slots(phase, q, k):
            n = step(phase, q, k)
            if phase < 2:
                return hi[:, k % RING, :], lo[:, k % RING, :], n - RING + 1
            free = n - 2 * RING + 1
            if isinstance(q, int):
                free = max(free, min(n - RING + 1, 2 * STEPS))
            return hi_wide[:, k % (2 * RING), :], lo_wide[:, k % (2 * RING), :], free

        params_loaded = sem("params_loaded")
        w_loaded = sem("w_loaded")
        x_loaded = [sem(f"x_loaded{i}") for i in range(2 * NG)]
        a_loaded = [sem(f"a_loaded{i}") for i in range(A_STAGE)]
        ident_made = sem("ident_made")
        ident_zeroed = sem("ident_zeroed")
        ones_made = sem("ones_made")
        a_rowsummed = sem("a_rowsummed")
        bank_filled = [sem(f"bank_filled{i}") for i in range(GROUP)]
        bank_drained = [sem(f"bank_drained{i}") for i in range(GROUP)]
        w_stat = sem("w_stat")
        w_total = sem("w_total")
        w_mean = sem("w_mean")
        var_made = sem("var_made")
        root_made = sem("root_made")
        norm_made = sem("norm_made")
        g_made = sem("g_made")
        wq_made = sem("wq_made")
        link_sem = sem("link_sem")
        b_loaded = [sem(f"b_loaded{i}") for i in range(STAGE)]
        b_formed = sem("b_formed")
        hi_made = sem("hi_made")
        lo_made = sem("lo_made")
        vhi_made = sem("vhi_made")
        vlo_made = sem("vlo_made")
        steps_done = sem("steps_done")
        acc_ready = sem("acc_ready")
        acc_drained = sem("acc_drained")
        u_made = sem("u_made")
        u_stored = sem("u_stored")
        u_loaded = [sem(f"u_loaded{i}") for i in range(NG)]
        xr_loaded = [sem(f"xr_loaded{i}") for i in range(GROUP)]
        x1_stored = [sem(f"x1_stored{i}") for i in range(GROUP)]
        x1_loaded = [sem(f"x1_loaded{i}") for i in range(GROUP)]
        out_stored = [sem(f"out_stored{i}") for i in range(GROUP)]
        h2_made = sem("h2_made")
        h2q_made = sem("h2q_made")
        h2qT_ready = sem("h2qT_ready")
        h2qT_made = sem("h2qT_made")
        sup_ready = sem("sup_ready")
        sup_made = sem("sup_made")
        sq_widened_act = sem("sq_widened_act")
        sq_widened_dve = sem("sq_widened_dve")
        sq_made = sem("sq_made")

        root_weights = NG + 1
        root_block = root_weights + 1

        block = ctx.enter_context(nc.Block())

        @block.sync
        def _(sp):
            sp.sem_inc(u_stored, FREE * 16)
            for n, (rg, cg) in enumerate(PIECES):
                for half in X_BEFORE.get(n, ()):
                    sp.dma_start(vec[:, half_blocks(half), :], x_rows[:, half_blocks(half), :]
                                 ).then_inc(x_loaded[half], 16)
                before = n - A_STAGE
                wait_for(sp, bank_filled[GROUP - 1], before + 1)
                wait_for(sp, a_rowsummed, before + 1)
                if before in HELD:
                    sp.wait_ge(b_formed, GROUP * (HELD.index(before) + 1))
                sp.dma_start(a_stage[:, n % A_STAGE, :, :],
                             adj_rows[:, rg * GROUP:(rg + 1) * GROUP, cg * GC:(cg + 1) * GC]
                             ).then_inc(a_loaded[n % A_STAGE], 16)
            sp.wait_ge(bank_filled[GROUP - 1], len(PIECES) - 1)
            sp.wait_ge(a_rowsummed, len(PIECES) - 1)

            def load_b(q):
                for k in range(NB):
                    sp.wait_ge(hi_made, step(0, q, k) - STAGE + 1)
                    sp.wait_ge(lo_made, step(0, q, k) - STAGE + 1)
                    sp.dma_start(b_stage[:, k % STAGE, :],
                                 adj_rows[:, k, bass.ds(q * GC, GC)]).then_inc(b_loaded[k % STAGE], 16)
                    if k == 7:
                        store_u(q - 1)

            def store_u(q):
                sp.wait_ge(u_made, GROUP * (q + 1))
                sp.dma_start(u_rows[:, bass.ds(q * GROUP, GROUP), :], rows[:, :, :]).then_inc(u_stored, 16)

            with sp.Fori(1, NG) as q:
                load_b(q)
            sp.dma_start(w_sb[:, :, :], w_rows).then_inc(w_loaded, 16)
            for g in range(NG - 1):
                sp.wait_ge(vlo_made, step(0, NG - 1, GROUP * (g + 1)))
                sp.wait_ge(vhi_made, step(0, NG - 1, GROUP * (g + 1)))
                if g == 0:
                    sp.wait_ge(u_stored, 16 * (FREE + NG - 1))
                sp.dma_start(vec[:, g * GROUP:(g + 1) * GROUP, :],
                             u_rows[:, g * GROUP:(g + 1) * GROUP, :]).then_inc(u_loaded[g], 16)
            store_u(NG - 1)
            sp.wait_ge(u_stored, 16 * (FREE + NG))
            sp.wait_ge(vlo_made, STEPS)
            sp.wait_ge(vhi_made, STEPS)
            sp.dma_start(vec[:, NB - GROUP:NB, :], u_rows[:, NB - GROUP:NB, :]).then_inc(u_loaded[NG - 1], 16)

            for j in range(GROUP):
                sp.dma_start(rows[:, j, :], x_rows[:, j, :]).then_inc(xr_loaded[j], 16)

            def store_x1(q):
                for j in range(GROUP):
                    sp.wait_ge(acc_drained, GROUP * (NG + q) + j + 1)
                    sp.dma_start(x1_rows[:, bass.ds(q * GROUP + j, 1), :], rows[:, j:j + 1, :]
                                 ).then_inc(x1_stored[j], 16)

            with sp.Fori(1, NG) as q:
                store_x1(q - 1)
                for j in range(GROUP):
                    sp.wait_ge(sq_made, GROUP * (q - 1) + j + 1)
                    sp.dma_start(rows[:, j:j + 1, :], x_rows[:, bass.ds(q * GROUP + j, 1), :]
                                 ).then_inc(xr_loaded[j], 16)
            store_x1(NG - 1)

            for j in range(GROUP):
                sp.wait_ge(sq_made, GROUP * (NG - 1) + j + 1)
                sp.wait_ge(x1_stored[j], 16 * NG)
                sp.dma_start(rows[:, j, :], x1_rows[:, j, :]).then_inc(x1_loaded[j], 16)

            def store_out(q):
                for j in range(GROUP):
                    sp.wait_ge(acc_drained, GROUP * (2 * NG + q) + j + 1)
                    sp.dma_start(out_rows[:, bass.ds(q * GROUP + j, 1), :], rows[:, j:j + 1, :]
                                 ).then_inc(out_stored[j], 16)

            with sp.Fori(1, NG) as q:
                store_out(q - 1)
                for j in range(GROUP):
                    sp.wait_ge(out_stored[j], 16 * q)
                    sp.dma_start(rows[:, j:j + 1, :], x1_rows[:, bass.ds(q * GROUP + j, 1), :]
                                 ).then_inc(x1_loaded[j], 16)
            store_out(NG - 1)
            for j in range(GROUP):
                sp.wait_ge(out_stored[j], 16 * NG)

        @block.gpsimd
        def _(pool):
            nc.gpsimd.memset(ident32[:, :], 0.0).then_inc(ident_zeroed, 1)
            nc.gpsimd.memset(ident16[:, :], 0.0).then_inc(ident_zeroed, 1)
            nc.gpsimd.memset(ones[:, :], 1.0).then_inc(ones_made, 1)
            pool.wait_ge(ident_zeroed, 2)
            for m in (ident32, ident16):
                nc.gpsimd.affine_select(out=m[:, :], in_=m[:, :], compare_op=ALU.not_equal, fill=1.0,
                                        base=0, pattern=[[-1, P]], channel_multiplier=1
                                        ).then_inc(ident_made, 1)

            def split_step(n, s, k):
                pool.wait_ge(vhi_made, n + 1)
                wait_for(pool, steps_done, n - RING + 1)
                nc.gpsimd.tensor_tensor(vlo[:, s % RING, :], vec[:, k, :], vhi32[:, s % RING, :],
                                        ALU.subtract).then_inc(vlo_made, 1)

            def split_low(phase, q):
                for k in range(NB):
                    split_step(step(phase, q, k), k, k)

            def form_held(n):
                shell, r = n // GROUP, n % GROUP
                piece = HELD[shell]
                if r == 0:
                    pool.wait_ge(a_loaded[piece % A_STAGE], 16 * (piece // A_STAGE + 1))
                    if shell > 1:
                        pool.wait_ge(a_rowsummed, piece + 1)
                        pool.wait_ge(bank_filled[GROUP - 1], piece + 1)
                    for kk in range(GROUP):
                        pool.wait_ge(bank_drained[kk], piece if shell < NG - 1 else piece + 1)
                if shell == 1:
                    pool.wait_ge(hi_made, r + 1)
                    pool.wait_ge(lo_made, r + 1)
                nc.gpsimd.tensor_tensor(held(n), a_stage[:, piece % A_STAGE, r, :],
                                        adjT[:, FIRST_K[n], 0:GC], ALU.add).then_inc(b_formed, 1)

            for what, n in walk(POOL_ORDER):
                if what == "F":
                    form_held(n)
                else:
                    split_step(n, n, FIRST_K[n])
            with pool.Fori(1, NG) as q:
                split_low(0, q)
            for phase in range(1, 2):
                split_low(phase, 0)
                with pool.Fori(1, NG) as q:
                    split_low(phase, q)

            pool.wait_ge(lo_made, 2 * STEPS)
            for k in range(NB):
                hi_slot, lo_slot, free = slots(2, 0, k)
                pool.wait_ge(hi_made, step(2, 0, k) + 1)
                pool.wait_ge(steps_done, free)
                nc.gpsimd.tensor_tensor(lo_slot, adjT[:, k, 0:GC], hi_slot.bitcast(F32), ALU.subtract
                                        ).then_inc(lo_made, 1)

        @block.scalar
        def _(act):
            act.sem_inc(h2qT_made, FREE)
            act.sem_inc(sup_made, FREE)
            act.wait_ge(ones_made, 1)
            nc.scalar.activation(first_root[:, :], ones[:, 0:1], ACT.Sqrt)
            act.dma_start(par[:, :], params[:, :]).then_inc(params_loaded, 16)

            def take_root(count, width):
                act.wait_ge(var_made, count)
                nc.scalar.activation(root[:, 0:width], var_[:, 0:width], ACT.Sqrt).then_inc(root_made, 1)

            def drain_piece(n):
                rg, cg = PIECES[n]
                if n == len(PIECES) - 1:
                    act.wait_ge(lo_made, 2 * GROUP)
                for kk in range(GROUP):
                    kb = cg * GROUP + kk
                    act.wait_ge(bank_filled[kk], n + 1)
                    nc.scalar.activation(adjT[:, kb, rg * GC:(rg + 1) * GC], bank[kk][:, :], ACT.Copy,
                                         accum_out=parts[:, NG + rg, kb:kb + 1]
                                         ).then_inc(bank_drained[kk], 1)

            def split_first(n):
                if n % GROUP == 0:
                    act.wait_ge(norm_made, n // GROUP + 1)
                k = FIRST_K[n]
                nc.scalar.activation(vec[:, k, :], vec[:, k, :], ACT.Relu, bias=gbias[:, k:k + 1],
                                     scale=gscale[:, k:k + 1]).then_inc(g_made, 1)
                act.wait_ge(g_made, n + 1)
                wait_for(act, steps_done, n - RING + 1)
                nc.scalar.activation(vhi[:, n % RING, :], vec[:, k, :], ACT.Copy
                                     ).then_inc(vhi_made, 1)
                act.wait_ge(b_formed, n + 1)
                nc.scalar.activation(hi[:, n % RING, :], held(n), ACT.Copy).then_inc(hi_made, 1)

            for what, n in walk(ACT_ORDER):
                if what == "P":
                    drain_piece(n)
                elif what == "D":
                    take_root(n + 1, 2 * GROUP)
                else:
                    split_first(n)

            def split_high(phase, q, k):
                n = step(phase, q, k)
                hi_slot, _, free = slots(phase, q, k)
                wait_for(act, steps_done, free)
                if phase < 2:
                    if phase == 1 and isinstance(q, int) and k % GROUP == 0:
                        act.wait_ge(u_loaded[k // GROUP], 16)
                    nc.scalar.activation(vhi[:, k % RING, :], vec[:, k, :], ACT.Copy).then_inc(vhi_made, 1)
                if phase == 0:
                    act.wait_ge(b_formed, n + 1)
                    piece = b_stage[:, k % STAGE, :]
                else:
                    piece = adjT[:, k, bass.ds(q * GC, GC)]
                nc.scalar.activation(hi_slot, piece, ACT.Copy).then_inc(hi_made, 1)

            def weight_sums(k):
                if k < DC:
                    if k == 0:
                        act.wait_ge(w_loaded, 16)
                    wait_for(act, w_stat, k)
                    nc.scalar.activation(bank[3][:, :], w_sb[:, k, :], ACT.Copy,
                                         accum_out=wst[:, k:k + 1]).then_inc(w_stat, 1)
                elif 6 <= k < 6 + DC:
                    if k == 6:
                        act.wait_ge(w_mean, 1)
                    act.wait_ge(w_stat, DC + k - 6)
                    nc.scalar.activation(bank[3][:, :], w_sb[:, k - 6, :], ACT.Square,
                                         bias=wst[:, 2 * DC:2 * DC + 1],
                                         accum_out=wst[:, DC + k - 6:DC + k - 5]).then_inc(w_stat, 1)
                elif k == 11:
                    take_root(root_weights, 1)

            def widen(k):
                if k == 0:
                    act.wait_ge(vlo_made, 2 * STEPS)
                act.wait_ge(sq_made, k + 1)
                nc.scalar.activation(sq_wide[:, k, :], sq[:, k, :], ACT.Copy).then_inc(sq_widened_act, 1)

            def chain(g, j, part):
                i = g * GROUP + j
                if part == 0:
                    take_root(root_block + i, 1)
                elif part == 1:
                    act.wait_ge(norm_made, NG + 1 + i)
                    act.wait_ge(x1_stored[j], 16 * (g + 1))
                    nc.scalar.activation(rows[:, j, :], rows[:, j, :], ACT.Relu, bias=nbias[:, 0:1],
                                         scale=rs[:, 0:1]).then_inc(h2_made, 1)
                elif part == 2:
                    act.wait_ge(h2qT_ready, i + FREE + 1)
                    act.wait_ge(sup_ready, i + FREE)
                    nc.scalar.activation(h2qT[:, :, :], t16[:, 0:D].rearrange("p (c r) -> p c r", c=DC),
                                         ACT.Copy).then_inc(h2qT_made, 1)
                else:
                    act.wait_ge(sup_ready, i + FREE + 1)
                    nc.scalar.activation(rows[:, j, :], sup[:, :], ACT.Relu, scale=delta[:, 2:3]
                                         ).then_inc(sup_made, 1)

            def group(phase, q, plan, g=None):
                for k in range(NB):
                    if phase == 2 and isinstance(q, int) and k < NB // 2:
                        widen(k)
                    split_high(phase, q, k)
                    if phase == 1 and isinstance(q, int):
                        weight_sums(k)
                    for j, part in plan.get(k, ()):
                        chain(g, j, part)

            with act.Fori(1, NG) as q:
                group(0, q, {})
            group(1, 0, {})
            with act.Fori(1, NG) as q:
                group(1, q, plans["act"], q - 1)
            group(2, 0, plans["act"], NG - 1)
            with act.Fori(1, NG) as q:
                group(2, q, {})

        @block.vector
        def _(dve):
            links = [0, 0]

            rounds = [0]

            def link(ins):
                links[1] += 1
                ins.then_inc(link_sem, 1)
                dve.wait_ge(link_sem, rounds[0] + links[0] + links[1])

            def links_close(times, per=None):
                assert per is None or links[1] == per, links
                links[0] += links[1] * times
                links[1] = 0
                rounds[0] = 0

            def rsqrt(width, requests):
                v, y, a = var_[:, 0:width], rs[:, 0:width], newton[:, 0:width]
                dve.wait_ge(root_made, requests)
                link(nc.vector.reciprocal(y, root[:, 0:width]))
                if width == 1:
                    link(nc.vector.scalar_tensor_tensor(out=a, in0=y, scalar=v, in1=y,
                                                        op0=ALU.mult, op1=ALU.mult))
                else:
                    link(nc.vector.tensor_tensor(a, y, v, ALU.mult))
                    link(nc.vector.tensor_tensor(a, a, y, ALU.mult))
                link(nc.vector.tensor_scalar(a, a, -0.5, 1.5, ALU.mult, ALU.add))
                link(nc.vector.tensor_tensor(y, y, a, ALU.mult))

            dve.wait_ge(params_loaded, 16)
            link(nc.vector.reciprocal(ipar[:, :], par[:, :]))
            link(nc.vector.tensor_scalar(delta[:, 0:1], par[:, 2:3], 1.0 / ACT_LEVELS, None, ALU.mult))
            link(nc.vector.tensor_scalar(delta[:, 1:2], par[:, 1:2], 1.0 / WGT_LEVELS, None, ALU.mult))
            link(nc.vector.tensor_tensor(delta[:, 2:3], delta[:, 0:1], delta[:, 1:2], ALU.mult))
            link(nc.vector.tensor_scalar(delta[:, 3:4], par[:, 3:4], 1.0 / ACT_LEVELS, None, ALU.mult))
            link(nc.vector.tensor_tensor(kappa[:, :], par[:, 0:1], ipar[:, 0:1], ALU.mult))
            link(nc.vector.tensor_tensor(kappa[:, :], kappa[:, :], delta[:, 3:4], ALU.mult))
            link(nc.vector.tensor_scalar(levels[:, :], ipar[:, 2:4], ACT_LEVELS, None, ALU.mult))
            links_close(1)

            def sum_piece(n):
                rg, cg = PIECES[n]
                dve.wait_ge(a_loaded[n % A_STAGE], 16 * (n // A_STAGE + 1))
                nc.vector.tensor_reduce(out=parts[:, cg, rg * GROUP:(rg + 1) * GROUP],
                                        in_=a_stage[:, n % A_STAGE, :, :], op=ALU.add, axis=AX_X
                                        ).then_inc(a_rowsummed, 1)

            def statistics(half):
                dve.wait_ge(x_loaded[half], 16)
                mine = half_blocks(half)
                for k in range(mine.start, mine.stop):
                    ins = nc.vector.bn_stats(out=stats[:, k % GROUP, :], in_=vec[:, k, :])
                link(ins)
                for k in range(mine.start, mine.stop):
                    ins = nc.vector.bn_aggr(out=mv[:, k, :], in_=stats[:, k % GROUP, :])
                link(ins)

            def degrees(shell):
                blocks = slice(SHELLS[shell] * GROUP, (SHELLS[shell] + 1) * GROUP)
                deg_t = deg[:, blocks]
                dve.wait_ge(a_rowsummed, HELD[shell] + 1)
                for b in range(GROUP):
                    dve.wait_ge(bank_drained[b], HELD[shell] + 1)
                link(nc.vector.tensor_reduce(out=deg_t, in_=parts[:, :, blocks].rearrange("p c b -> p b c"),
                                             op=ALU.add, axis=AX_X))
                link(nc.vector.tensor_scalar(deg_t, deg_t, 0.5, 1.0, ALU.mult, ALU.add))
                link(nc.vector.tensor_scalar(var_[:, 0:GROUP], mv[:, blocks, 1], LN_EPS, None, ALU.add))
                nc.vector.tensor_scalar(var_[:, GROUP:2 * GROUP], deg_t, TINY, None, ALU.max
                                        ).then_inc(var_made, 1)
                rsqrt(2 * GROUP, shell + 1)
                link(nc.vector.scalar_tensor_tensor(out=dinv[:, blocks], in0=deg_t, scalar=0.0,
                                                    in1=rs[:, GROUP:2 * GROUP], op0=ALU.is_gt, op1=ALU.mult))
                link(nc.vector.tensor_tensor(gscale[:, blocks], rs[:, 0:GROUP], dinv[:, blocks], ALU.mult))
                nc.vector.scalar_tensor_tensor(out=gbias[:, blocks], in0=mv[:, blocks, 0], scalar=-1.0,
                                               in1=gscale[:, blocks], op0=ALU.mult, op1=ALU.mult
                                               ).then_inc(norm_made, 1)

            def split_first(n):
                dve.wait_ge(hi_made, n + 1)
                wait_for(dve, steps_done, n - RING + 1)
                nc.vector.tensor_tensor(lo[:, n % RING, :], held(n), hi[:, n % RING, :].bitcast(F32),
                                        ALU.subtract).then_inc(lo_made, 1)

            for what, n in walk(DVE_ORDER):
                if what == "P":
                    sum_piece(n)
                elif what == "X":
                    statistics(n)
                elif what == "D":
                    degrees(n)
                else:
                    split_first(n)
            links_close(1)

            def weights(k):
                mean, total, wf = wst[:, 2 * DC:2 * DC + 1], wst[:, 2 * DC + 1:2 * DC + 2], w_sb[:, :, :]
                if k == 5:
                    dve.wait_ge(w_total, 1)
                    link(nc.vector.tensor_reduce(out=total, in_=bank[0][:, 0:DC], op=ALU.add, axis=AX_X))
                    nc.vector.tensor_scalar(mean, total, -1.0 / (D * D), None, ALU.mult
                                            ).then_inc(w_mean, 1)
                elif k == 11:
                    dve.wait_ge(w_total, 2)
                    link(nc.vector.tensor_reduce(out=total, in_=bank[0][:, DC:2 * DC], op=ALU.add, axis=AX_X))
                    nc.vector.tensor_scalar(var_[:, 0:1], total, 1.0 / (D * D - 1), None, ALU.mult
                                            ).then_inc(var_made, 1)
                elif k == 12:
                    rsqrt(1, root_weights)
                    link(nc.vector.tensor_scalar(wf, wf, mean, rs[:, 0:1], ALU.add, ALU.mult))
                elif k == 13:
                    link(nc.vector.tensor_scalar(wf, wf, ipar[:, 1:2], 1.0, ALU.mult, ALU.min))
                elif k == 14:
                    link(nc.vector.tensor_scalar(wf, wf, -1.0, WGT_LEVELS, ALU.max, ALU.mult))
                elif k == 15:
                    nc.vector.tensor_scalar(wq[:, :, :], wf, ROUND, -ROUND, ALU.add, ALU.add
                                            ).then_inc(wq_made, 1)

            def form_b(q, k):
                dve.wait_ge(b_loaded[k % STAGE], 16 * ((q - 1) * (NB // STAGE) + k // STAGE + 1))
                nc.vector.tensor_tensor(b_stage[:, k % STAGE, :], b_stage[:, k % STAGE, :],
                                        adjT[:, k, bass.ds(q * GC, GC)], ALU.add).then_inc(b_formed, 1)

            def split_low(phase, q, k):
                hi_slot, lo_slot, free = slots(phase, q, k)
                piece = b_stage[:, k % STAGE, :] if phase == 0 else adjT[:, k, bass.ds(q * GC, GC)]
                dve.wait_ge(hi_made, step(phase, q, k) + 1)
                wait_for(dve, steps_done, free)
                nc.vector.tensor_tensor(lo_slot, piece, hi_slot.bitcast(F32), ALU.subtract
                                        ).then_inc(lo_made, 1)

            def wait_bank(phase, q, b):
                if b < GROUP - 1:
                    dve.wait_ge(acc_ready, (GROUP - 1) * (phase * NG + q) + b + 1)
                else:
                    dve.wait_ge(steps_done, step(phase, q, NB))

            def drain(phase, q, banks):
                for b in banks:
                    wait_bank(phase, q, b)
                    if phase == 0:
                        if b == 0:
                            dve.wait_ge(u_stored, 16 * (q + FREE))
                        nc.vector.scalar_tensor_tensor(
                            out=rows[:, b:b + 1, :], in0=acc[:, b:b + 1, :], scalar=0.5,
                            in1=vec[:, bass.ds(q * GROUP + b, 1), :],
                            op0=ALU.mult, op1=ALU.add).then_inc(acc_drained, 1)
                    elif phase == 1:
                        dve.wait_ge(xr_loaded[b], 16 * (q + 1))
                        nc.vector.tensor_tensor(rows[:, b, :], rows[:, b, :], acc[:, b, :], ALU.add
                                                ).then_inc(acc_drained, 1)
                    else:
                        dve.wait_ge(x1_loaded[b], 16 * (q + 1))
                        nc.vector.scalar_tensor_tensor(
                            out=rows[:, b, :], in0=acc[:, b, :], scalar=kappa[:, 0:1], in1=rows[:, b, :],
                            op0=ALU.mult, op1=ALU.add).then_inc(acc_drained, 1)

            def scale_u(q, banks):
                for b in banks:
                    dve.wait_ge(acc_drained, GROUP * q + b + 1)
                    nc.vector.tensor_scalar(rows[:, b, :], rows[:, b, :], dinv[:, bass.ds(q * GROUP + b, 1)],
                                            None, ALU.mult).then_inc(u_made, 1)

            def quantise(tile, inverse, result):
                link(nc.vector.tensor_scalar(tile, tile, inverse, ACT_LEVELS, ALU.mult, ALU.min))
                return nc.vector.tensor_scalar(result, tile, ROUND, -ROUND, ALU.add, ALU.add)

            def chain(g, j, part):
                i = g * GROUP + j
                if part == 0:
                    dve.wait_ge(acc_drained, NG * GROUP + i + 1)
                    nc.vector.bn_stats(out=stats[:, 0, :], in_=rows[:, j, :])
                    dve.drain()
                    link(nc.vector.bn_aggr(out=mv[:, 0, :], in_=stats[:, 0, :]))
                    nc.vector.tensor_scalar(var_[:, 0:1], mv[:, 0, 1:2], LN_EPS, None, ALU.add
                                            ).then_inc(var_made, 1)
                elif part == 1:
                    rsqrt(1, root_block + i)
                    nc.vector.scalar_tensor_tensor(out=nbias[:, 0:1], in0=mv[:, 0, 0:1], scalar=-1.0,
                                                   in1=rs[:, 0:1], op0=ALU.mult, op1=ALU.mult
                                                   ).then_inc(norm_made, 1)
                elif part == 2:
                    dve.wait_ge(h2_made, i + 1)
                    dve.wait_ge(h2qT_ready, i + FREE)
                    quantise(rows[:, j, :], levels[:, 0:1], h2q[:, :]).then_inc(h2q_made, 1)
                else:
                    dve.wait_ge(sup_made, i + FREE + 1)
                    quantise(rows[:, j:j + 1, :], levels[:, 1:2], sq[:, bass.ds(i, 1), :]
                             ).then_inc(sq_made, 1)

            def group(phase, q, drained, plan, g=None):
                rounds[0] = 0 if isinstance(q, int) or not plan else (q - 1) * LINKS_CHAINS
                for k in range(0, NB, 2):
                    if phase == 0:
                        form_b(q, k)
                        form_b(q, k + 1)
                    if k == 0 and drained and phase < 2:
                        drain(*drained, [0])
                    own_low = phase < 2 or not isinstance(q, int)
                    if phase == 2 and not own_low:
                        widen(k)
                    if own_low:
                        split_low(phase, q, k)
                    if k == 0 and drained:
                        drain(*drained, range(1 if phase < 2 else 0, GROUP))
                    for j, part in plan.get(k, ()):
                        chain(g, j, part)
                    if phase == 1 and isinstance(q, int):
                        weights(k)
                    if own_low:
                        split_low(phase, q, k + 1)
                    if phase == 1 and isinstance(q, int):
                        weights(k + 1)
                    if k < GROUP and drained and drained[0] == 0:
                        scale_u(drained[1], (k, k + 1))
                    for j, part in plan.get(k + 1, ()):
                        chain(g, j, part)

            def widen(k):
                if k == 4:
                    dve.wait_ge(vlo_made, 2 * STEPS)
                    dve.wait_ge(vhi_made, 2 * STEPS)
                for b in {4: range(8, 12), 10: (12,), 12: (13,), 14: (14,)}.get(k, ()):
                    widen_block(b)

            def widen_block(b):
                dve.wait_ge(sq_made, b + 1)
                nc.vector.tensor_copy(sq_wide[:, b, :], sq[:, b, :]).then_inc(sq_widened_dve, 1)

            with dve.Fori(1, NG) as q:
                group(0, q, (0, q - 1), {})
            group(1, 0, (0, NG - 1), {})
            links_close(1)
            with dve.Fori(1, NG) as q:
                group(1, q, (1, q - 1), plans["dve"], q - 1)
            links_close(NG - 1, LINKS_CHAINS)
            group(2, 0, (1, NG - 1), plans["dve"], NG - 1)
            links_close(1, LINKS_CHAINS)
            widen_block(NB - 1)
            dve.wait_ge(lo_made, 2 * STEPS + NB)
            with dve.Fori(1, NG) as q:
                group(2, q, (2, q - 1), {})
            drain(2, NG - 1, range(GROUP))

        @block.tensor
        def _(pe):
            pe.sem_inc(h2qT_ready, FREE)
            pe.sem_inc(sup_ready, FREE)
            pe.wait_ge(ones_made, 1)
            pe.wait_ge(ident_made, 2)

            def transpose_piece(n):
                pe.wait_ge(a_loaded[n % A_STAGE], 16 * (n // A_STAGE + 1))
                for kk in range(GROUP):
                    wait_for(pe, bank_drained[kk], n)
                    for r in range(GROUP):
                        ins = nc.tensor.transpose(bank[kk][:, r * P:(r + 1) * P],
                                                  a_stage[:, n % A_STAGE, r, kk * P:(kk + 1) * P],
                                                  ident32[:, :])
                    ins.then_inc(bank_filled[kk], 1)

            def mm_step(phase, q, k):
                n = step(phase, q, k)
                hi_slot, lo_slot, _ = slots(phase, q, k)
                pe.wait_ge(hi_made, n + 1)
                if phase < 2:
                    pe.wait_ge(vhi_made, n + 1)
                    pe.wait_ge(vlo_made, n + 1)
                    moving = vhi[:, k % RING, :]
                else:
                    if isinstance(q, int):
                        if k < NB // 2:
                            pe.wait_ge(sq_widened_act, k + 1)
                        else:
                            pe.wait_ge(sq_widened_dve, k - NB // 2 + 1)
                    moving = sq_wide[:, k, :]
                pe.wait_ge(lo_made, n + 1)
                first, last = k == 0, k == NB - 1
                for b in range(GROUP):
                    hi_b, lo_b = hi_slot[:, b * P:(b + 1) * P], lo_slot[:, b * P:(b + 1) * P]
                    if first:
                        wait_for(pe, acc_drained, GROUP * (phase * NG + q - 1) + b + 1)
                    nc.tensor.matmul(acc[:, b, :], hi_b, moving, start=first, stop=False)
                    if phase < 2:
                        nc.tensor.matmul(acc[:, b, :], hi_b, vlo[:, k % RING, :], start=False, stop=False)
                    ins = nc.tensor.matmul(acc[:, b, :], lo_b, moving, start=False, stop=last)
                    if b == GROUP - 1:
                        ins.then_inc(steps_done, 1)
                    elif last:
                        ins.then_inc(acc_ready, 1)

            def last_steps(q):
                last = step(2, q, NB)
                pe.wait_ge(hi_made, last)
                pe.wait_ge(lo_made, last)
                for b in range(GROUP):
                    for k in (NB - 2, NB - 1):
                        hi_slot, lo_slot, _ = slots(2, q, k)
                        nc.tensor.matmul(acc[:, b, :], hi_slot[:, b * P:(b + 1) * P], sq_wide[:, k, :],
                                         start=False, stop=False)
                        ins = nc.tensor.matmul(acc[:, b, :], lo_slot[:, b * P:(b + 1) * P], sq_wide[:, k, :],
                                               start=False, stop=k == NB - 1)
                        if b == GROUP - 1:
                            ins.then_inc(steps_done, 1)
                        elif k == NB - 1:
                            ins.then_inc(acc_ready, 1)

            def chain(i, part):
                if part == 2:
                    pe.wait_ge(h2q_made, i + 1)
                    pe.wait_ge(h2qT_made, i + FREE)
                    for c in range(DC):
                        ins = nc.tensor.transpose(t16[:, c * P:(c + 1) * P], h2q[:, c * P:(c + 1) * P],
                                                  ident16[:, :])
                    ins.then_inc(h2qT_ready, 1)
                elif part == 3:
                    pe.wait_ge(h2qT_made, i + FREE + 1)
                    pe.wait_ge(sup_made, i + FREE)
                    for c in range(DC):
                        ins = nc.tensor.matmul(sup[:, :], h2qT[:, c, :], wq[:, c, :],
                                               start=c == 0, stop=c == DC - 1)
                    ins.then_inc(sup_ready, 1)

            def group(phase, q, plan, g=None):
                for k in range(NB):
                    mm_step(phase, q, k)
                    if phase == 1 and isinstance(q, int) and k in (3, 9):
                        total_weights(1 + k // 6)
                    for j, part in plan.get(k, ()):
                        chain(g * GROUP + j, part)

            def total_weights(count):
                cols = slice((count - 1) * DC, count * DC)
                pe.wait_ge(w_stat, count * DC)
                nc.tensor.matmul(bank[0][:, cols], ones[:, :], wst[:, cols], start=True, stop=True
                                 ).then_inc(w_total, 1)

            for what, n in walk(PE_ORDER):
                if what == "P":
                    transpose_piece(n)
                else:
                    mm_step(0, 0, n)
            with pe.Fori(1, NG) as q:
                group(0, q, {})
            group(1, 0, {})
            pe.wait_ge(wq_made, 1)
            with pe.Fori(1, NG) as q:
                group(1, q, plans["pe"], q - 1)
            group(2, 0, plans["pe"], NG - 1)
            with pe.Fori(1, NG) as q:
                for k in range(NB - 2):
                    mm_step(2, q, k)
                last_steps(q)


_OUTS = [((2048, 512), "float32")]


def kernel(**inputs):
    import numpy as _np
    import concourse.bacc as _bacc
    from concourse import mybir as _mybir
    from concourse.bass_utils import run_bass_kernel_spmd as _run

    def scalar(name):
        return _np.asarray(inputs[name]).reshape(1, 1)

    params = _np.ascontiguousarray(_np.broadcast_to(_np.concatenate(
        [scalar("L1_gnn_adj_scaling_factor"), scalar("L1_gnn_wgt_alpha"), scalar("L1_gnn_act_alpha"),
         scalar("L1_gnn_act_alpha2")], axis=1), (P, 4)))
    given = {"x": inputs["x"], "adj": inputs["adj"], "weight": inputs["L1_gnn_weight"], "params": params}

    nc = _bacc.Bacc("TRN2", target_bir_lowering=False, num_devices=1)
    arrays, args = {}, []
    for name, a in given.items():
        a = _np.ascontiguousarray(a)
        arrays[f"in_{name}_dram"] = a
        args.append(nc.dram_tensor(f"in_{name}_dram", a.shape, _mybir.dt.from_np(a.dtype), kind="ExternalInput").ap())
    for i, (shape, dtype) in enumerate(_OUTS):
        dt = _mybir.dt.from_np(_np.dtype(dtype))
        args.append(nc.dram_tensor(f"out_{i}_dram", shape, dt, kind="ExternalOutput").ap())
    gnn_layers_kernel(nc, *args)
    r = _run(nc, [arrays], core_ids=[0])
    return r.results[0]["out_0_dram"]
```
